# Optimizing a Trainium2 kernel written in Bass

```python
import numpy as np
import jax
import jax.numpy as jnp

def _softmax(x, axis=-1):
    return jax.nn.softmax(x, axis=axis)

def _gelu(x):
    return jax.nn.gelu(x, approximate=True)

def _silu(x):
    return jax.nn.silu(x)

def _sigmoid(x):
    return jax.nn.sigmoid(x)

def _layernorm(x, axis=-1, eps=1e-05):
    m = jnp.mean(x, axis=axis, keepdims=True)
    v = jnp.var(x, axis=axis, keepdims=True)
    return (x - m) / jnp.sqrt(v + eps)

def _scatter_add(tgt, idx, src, axis=0):
    return tgt.at[idx].add(src)

def _segment_sum(src, seg, n):
    return jax.ops.segment_sum(src, seg, n)
kernel_name = 'mk_cond_resid_d2_seqx_r8_54fb96'

def setup_inputs(seed: int=0):
    np.random.seed(seed)
    _w = jnp.asarray

    def _rec_inputs():
        import jax
        import jax.numpy as jnp
        _rk = jax.random.key(seed)
        x = -0.000125 + 0.9999 * jax.random.normal(jax.random.fold_in(_rk, 1), (8, 256, 128), jnp.float32)
        _lenS = 256 - jax.random.randint(jax.random.fold_in(_rk, 7), (8,), 0, max(1, 256 // 4) + 1, jnp.int32)
        _lenS2 = 256 - jax.random.randint(jax.random.fold_in(_rk, 8), (8,), 0, max(1, 256 // 4) + 1, jnp.int32)
        cond_8 = jax.random.uniform(jax.random.fold_in(_rk, 11), (8, 8), jnp.float32, 0.0, 0.983423)
        return (x, cond_8)
    x, cond_8 = _rec_inputs()

    def _L0_cond_setup():
        import jax, jax.numpy as jnp
        import numpy as np
        B, S, D = (16, 256, 128)
        E, H = (8, 256)
        key = jax.random.key(seed)
        ks = jax.random.split(key, 8)
        scale = 0.02
        x = jax.random.normal(ks[0], (B, S, D), dtype=jnp.float32)
        opcode_onehot = jax.random.uniform(ks[1], (B, E), dtype=jnp.float32)
        W_up = jax.random.normal(ks[2], (E, H, D), dtype=jnp.float32) * scale
        b_up = jnp.zeros((E, H), dtype=jnp.float32)
        W_gate = jax.random.normal(ks[3], (E, H, D), dtype=jnp.float32) * scale
        b_gate = jnp.zeros((E, H), dtype=jnp.float32)
        W_down = jax.random.normal(ks[4], (E, D, H), dtype=jnp.float32) * scale
        b_down = jnp.zeros((E, D), dtype=jnp.float32)
        return {'x': x, 'opcode_onehot': opcode_onehot, 'W_up': W_up, 'b_up': b_up, 'W_gate': W_gate, 'b_gate': b_gate, 'W_down': W_down, 'b_down': b_down}
    _L0_cond_all = _L0_cond_setup()
    _L0_cond_in = {k: v for k, v in _L0_cond_all.items() if k in ('W_up', 'b_up', 'W_gate', 'b_gate', 'W_down', 'b_down')}
    del _L0_cond_all

    def _L1_cond_setup():
        import jax, jax.numpy as jnp
        import numpy as np
        TOP_K = 2
        NUM_MOE_LAYERS = 12

        def _gemma_mlp(x, gate_w, up_w, down_w):
            g = jnp.einsum('bsh,hi->bsi', x, gate_w)
            u = jnp.einsum('bsh,hi->bsi', x, up_w)
            return jnp.einsum('bsi,ih->bsh', jax.nn.gelu(g, approximate=True) * u, down_w)
        key = jax.random.key(seed)
        ks = jax.random.split(key, 8)
        B, S, H, I, E = (32, 32, 128, 512, 8)
        std = 0.02
        return {'x': jax.random.normal(ks[0], (B, S, H), jnp.float32), 'router_logits': jax.random.normal(ks[1], (B, E), jnp.float32), 'skill_gate': jax.random.normal(ks[2], (E, H, I), jnp.float32) * std, 'skill_up': jax.random.normal(ks[3], (E, H, I), jnp.float32) * std, 'skill_down': jax.random.normal(ks[4], (E, I, H), jnp.float32) * std, 'shared_gate': jax.random.normal(ks[5], (H, I), jnp.float32) * std, 'shared_up': jax.random.normal(ks[6], (H, I), jnp.float32) * std, 'shared_down': jax.random.normal(ks[7], (I, H), jnp.float32) * std}
    _L1_cond_all = _L1_cond_setup()
    _L1_cond_in = {k: v for k, v in _L1_cond_all.items() if k in ('skill_gate', 'skill_up', 'skill_down', 'shared_gate', 'shared_up', 'shared_down')}
    del _L1_cond_all
    return {'x': x, 'cond_8': cond_8, 'L0_cond_W_up': _L0_cond_in['W_up'], 'L0_cond_b_up': _L0_cond_in['b_up'], 'L0_cond_W_gate': _L0_cond_in['W_gate'], 'L0_cond_b_gate': _L0_cond_in['b_gate'], 'L0_cond_W_down': _L0_cond_in['W_down'], 'L0_cond_b_down': _L0_cond_in['b_down'], 'L1_cond_skill_gate': _L1_cond_in['skill_gate'], 'L1_cond_skill_up': _L1_cond_in['skill_up'], 'L1_cond_skill_down': _L1_cond_in['skill_down'], 'L1_cond_shared_gate': _L1_cond_in['shared_gate'], 'L1_cond_shared_up': _L1_cond_in['shared_up'], 'L1_cond_shared_down': _L1_cond_in['shared_down']}

def reference(x, cond_8, L0_cond_W_up, L0_cond_b_up, L0_cond_W_gate, L0_cond_b_gate, L0_cond_W_down, L0_cond_b_down, L1_cond_skill_gate, L1_cond_skill_up, L1_cond_skill_down, L1_cond_shared_gate, L1_cond_shared_up, L1_cond_shared_down):
    import jax
    import jax.numpy as jnp

    def _L0_cond_ref(x, opcode_onehot, W_up, b_up, W_gate, b_gate, W_down, b_down):
        import jax, jax.numpy as jnp
        import numpy as np
        B, S, D = (16, 256, 128)
        E, H = (8, 256)
        expert = jnp.argmax(opcode_onehot, axis=-1)
        wu, bu = (W_up[expert], b_up[expert])
        wg, bg = (W_gate[expert], b_gate[expert])
        wd, bd = (W_down[expert], b_down[expert])
        up = jnp.einsum('bsd,bhd->bsh', x, wu) + bu[:, None, :]
        gate = jnp.einsum('bsd,bhd->bsh', x, wg) + bg[:, None, :]
        hidden = jax.nn.silu(up) * gate
        out = jnp.einsum('bsh,bdh->bsd', hidden, wd) + bd[:, None, :]
        return out

    def _L1_cond_ref(x, router_logits, skill_gate, skill_up, skill_down, shared_gate, shared_up, shared_down):
        import jax, jax.numpy as jnp
        import numpy as np
        TOP_K = 2
        NUM_MOE_LAYERS = 12

        def _gemma_mlp(x, gate_w, up_w, down_w):
            g = jnp.einsum('bsh,hi->bsi', x, gate_w)
            u = jnp.einsum('bsh,hi->bsi', x, up_w)
            return jnp.einsum('bsi,ih->bsh', jax.nn.gelu(g, approximate=True) * u, down_w)
        B = x.shape[0]
        E = skill_gate.shape[0]
        rw = jax.nn.softmax(router_logits.astype(jnp.float32), axis=-1)
        w, sel = jax.lax.top_k(rw, TOP_K)
        w = w / w.sum(axis=-1, keepdims=True)
        w = w.astype(x.dtype)
        scale = 1.0 / NUM_MOE_LAYERS
        w = scale * w + (1.0 - scale) * jax.lax.stop_gradient(w)
        dense_w = jnp.zeros((B, E), x.dtype).at[jnp.arange(B)[:, None], sel].add(w)

        def step(acc, params):
            g, u, d, we = params
            return (acc + we[:, None, None] * _gemma_mlp(x, g, u, d), None)
        out, _ = jax.lax.scan(step, jnp.zeros_like(x), (skill_gate, skill_up, skill_down, dense_w.T))
        out = out + _gemma_mlp(x, shared_gate, shared_up, shared_down)
        return out
    x = x + _L0_cond_ref(x, cond_8, L0_cond_W_up, L0_cond_b_up, L0_cond_W_gate, L0_cond_b_gate, L0_cond_W_down, L0_cond_b_down)
    x = x + _L1_cond_ref(x, cond_8, L1_cond_skill_gate, L1_cond_skill_up, L1_cond_skill_down, L1_cond_shared_gate, L1_cond_shared_up, L1_cond_shared_down)
    return x

_drawn_inputs = setup_inputs


def setup_inputs(seed=0):
    import zlib

    import numpy as np

    out = dict(_drawn_inputs(seed))
    spreads = {'L0_cond_b_up': (0.0, 0.8), 'L0_cond_b_gate': (0.0, 0.8), 'L0_cond_b_down': (0.0, 0.1)}
    factors = {'L0_cond_W_up': 6.239,
     'L0_cond_W_gate': 6.192,
     'L0_cond_W_down': 5.636,
     'L1_cond_skill_gate': 6.609,
     'L1_cond_skill_up': 6.525,
     'L1_cond_skill_down': 6.519,
     'L1_cond_shared_gate': 4.709,
     'L1_cond_shared_up': 4.634,
     'L1_cond_shared_down': 4.623}
    for name, (base, spread) in spreads.items():
        noise = np.random.default_rng([zlib.crc32(name.encode()), seed]).standard_normal(out[name].shape)
        drawn = base * np.exp(spread * noise) if base else spread * noise
        out[name] = jnp.asarray(drawn.astype(out[name].dtype))
    for name, factor in factors.items():
        out[name] = (out[name] * factor).astype(out[name].dtype)
    return out
```

```python
from contextlib import ExitStack

import concourse.bass as bass
from concourse import mybir

F32 = mybir.dt.float32
F32R = mybir.dt.float32r
U32 = mybir.dt.uint32
ALU = mybir.AluOpType
ACT = mybir.ActivationFunctionType
AXX = mybir.AxisListType.X

B, S, D = 8, 256, 128
E, TOP_K = 8, 2
H0, H1 = 256, 512
P = 128
C0, C1 = H0 // P, H1 // P
SCALE = 1.0 / 12

UP0, GATE0, DOWN0 = 0, H0, 2 * H0
BUP0 = DOWN0 + C0 * D
BGATE0 = BUP0 + C0
BDOWN0 = BGATE0 + C0
W0 = BUP0
R0 = BDOWN0 + 1
GATE1, UP1, DOWN1 = 0, H1, 2 * H1
W1 = DOWN1 + C1 * D
GU1 = DOWN1

MLPS = TOP_K + 1
HALF = 2
STEPS = MLPS * C1 // HALF
RING = 3
LAG = RING - 1


TURNS = (B - LAG) // RING
assert TURNS * RING == B - LAG


def program(nc, x_t, cond, w0_packed, w1_packed, shared_packed, out_t):
    ctx = ExitStack()
    with ctx:
        def sb(name, shape, dt=F32):
            return ctx.enter_context(nc.sbuf_tensor(name, shape, dt))

        def ps(name):
            return ctx.enter_context(nc.psum_tensor(name, [P, 512], F32))

        def sem(name):
            return ctx.enter_context(nc.semaphore(name))

        cond_sb = sb("cond_sb", [P, B, E])
        top_v = sb("top_v", [P, B, E])
        top_i = sb("top_i", [P, B * E], U32)
        top_d = sb("top_d", [P, B, E])
        top_e = sb("top_e", [P, B, E])
        row_a = sb("row_a", [P, B])
        row_b = sb("row_b", [P, B])
        rw = sb("rw", [P, B, TOP_K])
        rw_n = sb("rw_n", [P, B, TOP_K])
        rw_t = sb("rw_t", [P, B, TOP_K])
        mix = sb("mix", [P, B * TOP_K])

        x = sb("x", [P, B * S])
        x_hi = sb("x_hi", [P, B * S], F32R)
        x_lo = sb("x_lo", [P, B * S], F32R)
        x1 = sb("x1", [P, B * S])
        x1_hi = sb("x1_hi", [P, B * S], F32R)
        x1_lo = sb("x1_lo", [P, B * S], F32R)

        w0_raw = sb("w0_raw", [P, B * R0])
        w0_hi = [sb(f"w0_hi{r}", [P, W0], F32R) for r in range(RING)]
        w0_lo = [sb(f"w0_lo{r}", [P, W0], F32R) for r in range(RING)]
        w1_raw = [sb(f"w1_raw{k}", [P, W1]) for k in range(MLPS)]
        w1_hi = [sb(f"w1_hi{k}", [P, W1], F32R) for k in range(MLPS)]
        w1_lo = [sb(f"w1_lo{k}", [P, W1], F32R) for k in range(MLPS)]

        act_h = [sb(f"act_h{r}", [P, HALF * S]) for r in range(RING)]
        h = [sb(f"h{r}", [P, HALF * S]) for r in range(RING)]
        h_hi = [sb(f"h_hi{r}", [P, HALF * S], F32R) for r in range(RING)]
        h_lo = [sb(f"h_lo{r}", [P, HALF * S], F32R) for r in range(RING)]

        act_ps = [ps(f"act_ps{r}") for r in range(RING)]
        mul_ps = [ps(f"mul_ps{r}") for r in range(RING)]
        out_ps = ps("out_ps")

        x_loaded = [sem(f"x_loaded{n}") for n in range(2)]
        w0_loaded = [sem(f"w0_loaded{r}") for r in range(RING)]
        w1_loaded = [sem(f"w1_loaded{k}") for k in range(MLPS)]
        routed = sem("routed")
        route_step = sem("route_step")
        top_d_done = sem("top_d_done")
        top_e_done = sem("top_e_done")
        x_hi_done = sem("x_hi_done")
        x_lo_done = sem("x_lo_done")
        w0_hi_done = sem("w0_hi_done")
        w0_lo_done = sem("w0_lo_done")
        act0_ready = sem("act0_ready")
        mul0_ready = sem("mul0_ready")
        silu_done = sem("silu_done")
        h0_done = sem("h0_done")
        h0_hi_done = sem("h0_hi_done")
        h0_lo_done = sem("h0_lo_done")
        out0_ready = sem("out0_ready")
        x1_done = sem("x1_done")
        x1_hi_done = sem("x1_hi_done")
        x1_lo_done = sem("x1_lo_done")
        w1_hi_done = sem("w1_hi_done")
        w1_gu_split = [sem(f"w1_gu_split{k}") for k in range(MLPS)]
        w1_d_split = [sem(f"w1_d_split{k}") for k in range(MLPS)]
        act_ready = sem("act_ready")
        mul_ready = sem("mul_ready")
        gelu_done = sem("gelu_done")
        h_done = sem("h_done")
        h_hi_done = sem("h_hi_done")
        h_lo_done = sem("h_lo_done")
        down_done = sem("down_done")
        y_done = sem("y_done")
        stored = sem("stored")
        cond_loaded = sem("cond_loaded")

        def row(t, b):
            return t[:, bass.ds(b * S, S)]

        def chunk(t, c):
            return t[:, c * S:(c + 1) * S]

        block = ctx.enter_context(nc.Block())

        @block.sync
        def _(sp):
            sp.dma_start(cond_sb[:, :, :].rearrange("p b e -> p (b e)"),
                         cond.partition_broadcast(P)).then_inc(cond_loaded, 16)

            for b in range(B):
                r, loads_before = b % RING, b // RING
                sp.wait_ge(routed, b + 1)
                if loads_before:
                    sp.wait_ge(w0_loaded[r], 16 * loads_before)
                expert = sp.value_load(top_i[0:1, b * E:b * E + 1], min_val=0, max_val=E - 1)
                sp.dma_start(w0_raw[:, b * R0:(b + 1) * R0],
                             w0_packed[bass.ds(expert, 1), :, :].rearrange("e p n -> (e p) n")
                             ).then_inc(w0_loaded[r], 16)

            def load1(b, k):
                if b:
                    sp.wait_ge(w1_d_split[k], b)
                expert = sp.value_load(top_i[0:1, b * E + k:b * E + k + 1], min_val=0, max_val=E - 1)
                sp.dma_start(w1_raw[k][:, :],
                             w1_packed[bass.ds(expert, 1), :, :].rearrange("e p n -> (e p) n")
                             ).then_inc(w1_loaded[k], 16)

            for b in range(B):
                for k in range(TOP_K):
                    load1(b, k)
                if b == 0:
                    sp.dma_start(w1_raw[TOP_K][:, :], shared_packed).then_inc(w1_loaded[TOP_K], 16)
                else:
                    sp.wait_ge(y_done, b)
                    sp.dma_start(out_t[:, (b - 1) * S:b * S], row(x, b - 1)).then_inc(stored, 16)
            sp.wait_ge(y_done, B)
            sp.dma_start(out_t[:, (B - 1) * S:B * S], row(x, B - 1)).then_inc(stored, 16)
            sp.wait_ge(stored, 16 * B)

        @block.gpsimd
        def _(pool):
            for b in range(B):
                r = b % RING
                pool.wait_ge(w0_loaded[r], 16 * (b // RING + 1))
                if b >= RING:
                    pool.wait_ge(out0_ready, b - RING + 1)
                for n, (lo, hi) in enumerate(((UP0, DOWN0), (DOWN0, W0))):
                    raw = w0_raw[:, b * R0 + lo:b * R0 + hi]
                    nc.gpsimd.tensor_copy(w0_hi[r][:, lo:hi], raw).then_inc(w0_hi_done, 1)
                    pool.wait_ge(w0_hi_done, 2 * b + n + 1)
                    nc.gpsimd.tensor_tensor(w0_lo[r][:, lo:hi], raw, w0_hi[r][:, lo:hi].bitcast(F32),
                                            ALU.subtract).then_inc(w0_lo_done, 1)

            pieces = 0
            for b in range(B):
                for k in range(TOP_K if b else MLPS):
                    pool.wait_ge(w1_loaded[k], 16 * (b + 1))
                    for lo, hi, split, used in ((0, GU1, w1_gu_split[k], mul_ready),
                                                (GU1, W1, w1_d_split[k], down_done)):
                        if b:
                            pool.wait_ge(used, (b - 1) * STEPS + 2 * (k + 1))
                        nc.gpsimd.tensor_copy(w1_hi[k][:, lo:hi], w1_raw[k][:, lo:hi]).then_inc(w1_hi_done, 1)
                        pieces += 1
                        pool.wait_ge(w1_hi_done, pieces)
                        nc.gpsimd.tensor_tensor(w1_lo[k][:, lo:hi], w1_raw[k][:, lo:hi],
                                                w1_hi[k][:, lo:hi].bitcast(F32), ALU.subtract).then_inc(split, 1)

        @block.scalar
        def _(act):
            act.dma_start(x[:, 0:S], x_t[:, 0:S]).then_inc(x_loaded[0], 16)
            act.dma_start(x[:, S:], x_t[:, S:]).then_inc(x_loaded[1], 16)
            act.wait_ge(top_d_done, 1)
            nc.scalar.activation(top_e[:, :, :], top_d[:, :, :], ACT.Exp).then_inc(top_e_done, 1)
            for n, (lo, hi) in enumerate(((0, S), (S, B * S))):
                act.wait_ge(x_loaded[n], 16)
                nc.scalar.copy(x_hi[:, lo:hi], x[:, lo:hi]).then_inc(x_hi_done, 1)

            def silu0(b, r, turn):
                act.wait_ge(w0_loaded[r], turn * 16 + 16)
                act.wait_ge(act0_ready, b + 1)
                for c in range(C0):
                    ins = nc.scalar.activation(chunk(act_h[r], c), chunk(act_ps[r], c), ACT.Silu,
                                               bias=w0_raw[:, bass.ds(b * R0 + BUP0 + c, 1)])
                ins.then_inc(silu_done, 1)

            def round_h0(b, r):
                act.wait_ge(h0_done, b + 1)
                nc.scalar.copy(h_hi[r][:, :], h[r][:, :]).then_inc(h0_hi_done, 1)

            silu0(0, 0, 0)
            with act.Fori(0, TURNS) as turn:
                for j in range(RING):
                    b = turn * RING + j
                    silu0(b + 1, (j + 1) % RING, turn + (j + 1) // RING)
                    round_h0(b, j)
            for b in range(TURNS * RING, B):
                if b + 1 < B:
                    silu0(b + 1, (b + 1) % RING, (b + 1) // RING)
                round_h0(b, b % RING)

            def gelu(n, r):
                act.wait_ge(act_ready, n + 1)
                nc.scalar.activation(act_h[r][:, :], act_ps[r][:, :], ACT.Gelu_apprx_tanh).then_inc(gelu_done, 1)

            def round_h(n, r):
                act.wait_ge(h_done, n + 1)
                nc.scalar.copy(h_hi[r][:, :], h[r][:, :]).then_inc(h_hi_done, 1)

            def layer1(b, last=False):
                for s in range(STEPS):
                    if not (last and s == STEPS - 1):
                        gelu(b * STEPS + s + 1, (s + 1) % RING)
                    round_h(b * STEPS + s, s % RING)

            gelu(0, 0)
            with act.Fori(0, B - 1) as b:
                layer1(b)
            layer1(B - 1, last=True)

        @block.vector
        def _(dve):
            dve.wait_ge(cond_loaded, 16)
            steps = [0]

            def step(ins):
                ins.then_inc(route_step, 1)
                steps[0] += 1
                dve.wait_ge(route_step, steps[0])

            for b in range(B):
                step(nc.vector.max(top_v[:, b, :], cond_sb[:, b, :]))
                nc.vector.max_index(top_i[:, b * E:(b + 1) * E], top_v[:, b, :], cond_sb[:, b, :]).then_inc(routed, 1)
            nc.vector.tensor_tensor(top_d[:, :, :], top_v[:, :, :], top_v[:, :, 0:1].to_broadcast([P, B, E]),
                                    ALU.subtract).then_inc(top_d_done, 1)
            dve.wait_ge(top_e_done, 1)
            step(nc.vector.reduce_sum(row_a[:, :], top_e[:, :, :], AXX))
            step(nc.vector.reciprocal(row_b[:, :], row_a[:, :]))
            step(nc.vector.tensor_tensor(rw[:, :, :], top_e[:, :, 0:TOP_K],
                                         row_b[:, :].unsqueeze(2).to_broadcast([P, B, TOP_K]), ALU.mult))
            step(nc.vector.reduce_sum(row_a[:, :], rw[:, :, :], AXX))
            step(nc.vector.reciprocal(row_b[:, :], row_a[:, :]))
            step(nc.vector.tensor_tensor(rw_n[:, :, :], rw[:, :, :],
                                         row_b[:, :].unsqueeze(2).to_broadcast([P, B, TOP_K]), ALU.mult))
            step(nc.vector.tensor_scalar(rw_t[:, :, :], rw_n[:, :, :], 1.0 - SCALE, None, ALU.mult))
            step(nc.vector.scalar_tensor_tensor(mix[:, :].rearrange("p (b k) -> p b k", k=TOP_K), rw_n[:, :, :],
                                                SCALE, rw_t[:, :, :], ALU.mult, ALU.add))

            for n, (lo, hi) in enumerate(((0, S), (S, B * S))):
                dve.wait_ge(x_hi_done, n + 1)
                nc.vector.tensor_tensor(x_lo[:, lo:hi], x[:, lo:hi], x_hi[:, lo:hi].bitcast(F32),
                                        ALU.subtract).then_inc(x_lo_done, 1)

            def product0(b, r):
                dve.wait_ge(mul0_ready, b + 1)
                dve.wait_ge(silu_done, b + 1)
                for c in range(C0):
                    ins = nc.vector.scalar_tensor_tensor(chunk(h[r], c), chunk(mul_ps[r], c),
                                                         w0_raw[:, bass.ds(b * R0 + BGATE0 + c, 1)],
                                                         chunk(act_h[r], c), ALU.add, ALU.mult)
                ins.then_inc(h0_done, 1)

            def rest_h0(b, r):
                dve.wait_ge(h0_hi_done, b + 1)
                nc.vector.tensor_tensor(h_lo[r][:, :], h[r][:, :], h_hi[r][:, :].bitcast(F32),
                                        ALU.subtract).then_inc(h0_lo_done, 1)

            def residual0(b):
                dve.wait_ge(out0_ready, b + 1)
                nc.vector.scalar_tensor_tensor(row(x1, b), out_ps[:, 0:S],
                                               w0_raw[:, bass.ds(b * R0 + BDOWN0, 1)],
                                               row(x, b), ALU.add, ALU.add).then_inc(x1_done, 1)
                dve.wait_ge(x1_done, b + 1)
                nc.vector.tensor_copy(row(x1_hi, b), row(x1, b)).then_inc(x1_hi_done, 1)
                dve.wait_ge(x1_hi_done, b + 1)
                nc.vector.tensor_tensor(row(x1_lo, b), row(x1, b), row(x1_hi, b).bitcast(F32),
                                        ALU.subtract).then_inc(x1_lo_done, 1)

            product0(0, 0)
            product0(1, 1)
            rest_h0(0, 0)
            with dve.Fori(0, TURNS) as turn:
                for j in range(RING):
                    b = turn * RING + j
                    product0(b + 2, (j + 2) % RING)
                    rest_h0(b + 1, (j + 1) % RING)
                    residual0(b)
            for b in range(TURNS * RING, B):
                if b + 1 < B:
                    rest_h0(b + 1, (b + 1) % RING)
                residual0(b)

            def product(n, b, s):
                r, k = s % RING, s * HALF // C1
                dve.wait_ge(mul_ready, n + 1)
                dve.wait_ge(gelu_done, n + 1)
                if k < TOP_K:
                    ins = nc.vector.scalar_tensor_tensor(h[r][:, :], act_h[r][:, :],
                                                         mix[:, bass.ds(b * TOP_K + k, 1)],
                                                         mul_ps[r][:, :], ALU.mult, ALU.mult)
                else:
                    ins = nc.vector.tensor_tensor(h[r][:, :], act_h[r][:, :], mul_ps[r][:, :], ALU.mult)
                ins.then_inc(h_done, 1)

            def rest_h(n, r):
                dve.wait_ge(h_hi_done, n + 1)
                nc.vector.tensor_tensor(h_lo[r][:, :], h[r][:, :], h_hi[r][:, :].bitcast(F32),
                                        ALU.subtract).then_inc(h_lo_done, 1)

            def residual1(b):
                dve.wait_ge(down_done, (b + 1) * STEPS)
                nc.vector.tensor_tensor(row(x, b), out_ps[:, 0:S], row(x1, b), ALU.add).then_inc(y_done, 1)

            def layer1(b, first=False, last=False):
                for s in range(STEPS):
                    if s == 1 and not first:
                        residual1(b - 1)
                    if s < STEPS - 1:
                        product(b * STEPS + s + 1, b, s + 1)
                    elif not last:
                        product((b + 1) * STEPS, b + 1, 0)
                    rest_h(b * STEPS + s, s % RING)

            product(0, 0, 0)
            layer1(0, first=True)
            with dve.Fori(1, B - 1) as b:
                layer1(b)
            layer1(B - 1, last=True)
            residual1(B - 1)

        @block.tensor
        def _(pe):
            def product3(out, w_hi, w_lo, m_hi, m_lo, start, stop):
                nc.tensor.matmul(out, w_hi, m_hi, start=start, stop=False)
                nc.tensor.matmul(out, w_hi, m_lo, start=False, stop=False)
                return nc.tensor.matmul(out, w_lo, m_hi, start=False, stop=stop)

            def up0(b, r):
                pe.wait_ge(w0_lo_done, b * 2 + 1)
                for ps_t, at, ready in ((act_ps, UP0, act0_ready), (mul_ps, GATE0, mul0_ready)):
                    for c in range(C0):
                        cols = slice(at + c * P, at + (c + 1) * P)
                        last = product3(chunk(ps_t[r], c), w0_hi[r][:, cols], w0_lo[r][:, cols],
                                        row(x_hi, b), row(x_lo, b), True, True)
                    last.then_inc(ready, 1)

            def down0(b, r):
                pe.wait_ge(w0_lo_done, b * 2 + 2)
                pe.wait_ge(h0_lo_done, b + 1)
                pe.wait_ge(x1_done, b)
                for c in range(C0):
                    cols = slice(DOWN0 + c * D, DOWN0 + (c + 1) * D)
                    last = product3(out_ps[:, 0:S], w0_hi[r][:, cols], w0_lo[r][:, cols],
                                    chunk(h_hi[r], c), chunk(h_lo[r], c), c == 0, c == C0 - 1)
                last.then_inc(out0_ready, 1)

            pe.wait_ge(x_lo_done, 1)
            up0(0, 0)
            pe.wait_ge(x_lo_done, 2)
            up0(1, 1)
            with pe.Fori(0, TURNS) as turn:
                for j in range(RING):
                    b = turn * RING + j
                    up0(b + LAG, (j + LAG) % RING)
                    down0(b, j)
            for b in range(TURNS * RING, B):
                down0(b, b % RING)

            def up1(n, b, s, first=False):
                r, k, half = s % RING, s * HALF // C1, s % (C1 // HALF)
                if s == 0:
                    pe.wait_ge(x1_lo_done, b + 1)
                if half == 0:
                    pe.wait_ge(w1_gu_split[k], b + 1 if k < TOP_K else 1)
                if not first:
                    pe.wait_ge(gelu_done, n - RING + 1)
                    pe.wait_ge(h_done, n - RING + 1)
                for ps_t, at, ready in ((act_ps, GATE1, act_ready), (mul_ps, UP1, mul_ready)):
                    for c in range(HALF):
                        lo = at + (half * HALF + c) * P
                        last = product3(chunk(ps_t[r], c), w1_hi[k][:, lo:lo + P], w1_lo[k][:, lo:lo + P],
                                        row(x1_hi, b), row(x1_lo, b), True, True)
                    last.then_inc(ready, 1)

            def down1(n, b, s):
                r, k, half = s % RING, s * HALF // C1, s % (C1 // HALF)
                if s == 0:
                    pe.wait_ge(y_done, b)
                if half == 0:
                    pe.wait_ge(w1_d_split[k], b + 1 if k < TOP_K else 1)
                pe.wait_ge(h_lo_done, n + 1)
                for c in range(HALF):
                    lo = DOWN1 + (half * HALF + c) * D
                    last = product3(out_ps[:, 0:S], w1_hi[k][:, lo:lo + D], w1_lo[k][:, lo:lo + D],
                                    chunk(h_hi[r], c), chunk(h_lo[r], c),
                                    s == 0 and c == 0, s == STEPS - 1 and c == HALF - 1)
                last.then_inc(down_done, 1)

            def layer1(b, first=False, last=False):
                for s in range(STEPS):
                    ahead = s + LAG
                    if ahead < STEPS:
                        up1(b * STEPS + ahead, b, ahead, first=first and ahead < RING)
                    elif not last:
                        up1((b + 1) * STEPS + ahead - STEPS, b + 1, ahead - STEPS)
                    down1(b * STEPS + s, b, s)

            for s in range(LAG):
                up1(s, 0, s, first=True)
            layer1(0, first=True)
            with pe.Fori(1, B - 1) as b:
                layer1(b)
            layer1(B - 1, last=True)


def kernel(x, cond_8, L0_cond_W_up, L0_cond_b_up, L0_cond_W_gate, L0_cond_b_gate, L0_cond_W_down, L0_cond_b_down,
           L1_cond_skill_gate, L1_cond_skill_up, L1_cond_skill_down,
           L1_cond_shared_gate, L1_cond_shared_up, L1_cond_shared_down):
    import numpy as np
    import concourse.bacc as bacc
    from concourse.bass_utils import run_bass_kernel_spmd

    def chunks_to_columns(w, parts):
        *lead, rows, n = w.shape
        w = w.reshape(*lead, parts, rows // parts, n)
        return np.moveaxis(w, -3, -2).reshape(*lead, rows // parts, parts * n)

    x_t = np.ascontiguousarray(np.asarray(x).reshape(B * S, D).T)
    cond = np.ascontiguousarray(np.asarray(cond_8).reshape(B * E))
    w0 = np.concatenate([
        np.swapaxes(np.asarray(L0_cond_W_up), 1, 2),
        np.swapaxes(np.asarray(L0_cond_W_gate), 1, 2),
        chunks_to_columns(np.swapaxes(np.asarray(L0_cond_W_down), 1, 2), C0),
        chunks_to_columns(np.asarray(L0_cond_b_up)[:, :, None], C0),
        chunks_to_columns(np.asarray(L0_cond_b_gate)[:, :, None], C0),
        np.asarray(L0_cond_b_down)[:, :, None],
    ], axis=-1)
    w1 = np.concatenate([np.asarray(L1_cond_skill_gate), np.asarray(L1_cond_skill_up),
                         chunks_to_columns(np.asarray(L1_cond_skill_down), C1)], axis=-1)
    shared = np.concatenate([np.asarray(L1_cond_shared_gate), np.asarray(L1_cond_shared_up),
                             chunks_to_columns(np.asarray(L1_cond_shared_down), C1)], axis=-1)
    arrays = {"x_t": x_t, "cond": cond, "w0": w0, "w1": w1, "shared": shared}
    arrays = {name: np.ascontiguousarray(a) for name, a in arrays.items()}

    nc = bacc.Bacc("TRN2", target_bir_lowering=False, num_devices=1)
    ins = [nc.dram_tensor(name, a.shape, mybir.dt.from_np(a.dtype), kind="ExternalInput").ap()
           for name, a in arrays.items()]
    out = nc.dram_tensor("out_t", (D, B * S), F32, kind="ExternalOutput").ap()
    program(nc, *ins, out)
    got = run_bass_kernel_spmd(nc, [arrays], core_ids=[0]).results[0]["out_t"]
    return np.ascontiguousarray(got.T).reshape(B, S, D)
```

```python
from contextlib import ExitStack

import concourse.bass as bass
from concourse import mybir

F32 = mybir.dt.float32
F32R = mybir.dt.float32r
U32 = mybir.dt.uint32
ALU = mybir.AluOpType
ACT = mybir.ActivationFunctionType
AXX = mybir.AxisListType.X

B, S, D = 8, 256, 128
E, TOP_K = 8, 2
H0, H1 = 256, 512
P = 128
C0, C1 = H0 // P, H1 // P
SCALE = 1.0 / 12

UP0, GATE0, DOWN0 = 0, H0, 2 * H0
BUP0 = DOWN0 + C0 * D
BGATE0 = BUP0 + C0
BDOWN0 = BGATE0 + C0
W0 = BUP0
R0 = BDOWN0 + 1
GATE1, UP1, DOWN1 = 0, H1, 2 * H1
W1 = DOWN1 + C1 * D
W0_PIECES = ((0, DOWN0), (DOWN0, W0))
W1_PIECES = ((0, DOWN1), (DOWN1, W1))

MLPS = TOP_K + 1
HALF = 2
STEPS = MLPS * C1 // HALF
RING = 3
LAG = 2


W0_RING = 4


def program(nc, x_t, cond, w0_packed, w1_packed, shared_packed, out_t):
    ctx = ExitStack()
    with ctx:
        def sb(name, shape, dt=F32):
            return ctx.enter_context(nc.sbuf_tensor(name, shape, dt))

        def ps(name):
            return ctx.enter_context(nc.psum_tensor(name, [P, 512], F32))

        def sem(name):
            return ctx.enter_context(nc.semaphore(name))

        cond_sb = sb("cond_sb", [P, B, E])
        top_v = sb("top_v", [P, B, E])
        top_i = sb("top_i", [P, B * E], U32)
        top_d = sb("top_d", [P, B, E])
        top_e = sb("top_e", [P, B, E])
        row_a = sb("row_a", [P, B])
        row_b = sb("row_b", [P, B])
        rw = sb("rw", [P, B, TOP_K])
        rw_n = sb("rw_n", [P, B, TOP_K])
        rw_t = sb("rw_t", [P, B, TOP_K])
        mix = sb("mix", [P, B * TOP_K])

        x = sb("x", [P, B * S])
        x_hi = sb("x_hi", [P, B * S], F32R)
        x_lo = sb("x_lo", [P, B * S], F32R)
        x1 = sb("x1", [P, B * S])
        x1_hi = sb("x1_hi", [P, B * S], F32R)
        x1_lo = sb("x1_lo", [P, B * S], F32R)

        w0_raw = sb("w0_raw", [P, B * R0])
        w0_hi = [sb(f"w0_hi{r}", [P, W0], F32R) for r in range(W0_RING)]
        w0_lo = [sb(f"w0_lo{r}", [P, W0], F32R) for r in range(W0_RING)]
        w1_raw = [sb(f"w1_raw{k}", [P, W1]) for k in range(MLPS)]
        w1_hi = [sb(f"w1_hi{k}", [P, W1], F32R) for k in range(MLPS)]
        w1_lo = [sb(f"w1_lo{k}", [P, W1], F32R) for k in range(MLPS)]

        act_h = [sb(f"act_h{r}", [P, HALF * S]) for r in range(RING)]
        h = [sb(f"h{r}", [P, HALF * S]) for r in range(RING)]
        h_hi = [sb(f"h_hi{r}", [P, HALF * S], F32R) for r in range(RING)]
        h_lo = [sb(f"h_lo{r}", [P, HALF * S], F32R) for r in range(RING)]

        act_ps = [ps(f"act_ps{r}") for r in range(RING)]
        mul_ps = [ps(f"mul_ps{r}") for r in range(RING)]
        out_ps = [ps(f"out_ps{j}") for j in range(2)]

        x_loaded = [sem(f"x_loaded{n}") for n in range(2)]
        w0_loaded = [sem(f"w0_loaded{r}") for r in range(RING)]
        w1_loaded = [sem(f"w1_loaded{k}") for k in range(MLPS)]
        routed = sem("routed")
        route_step = sem("route_step")
        top_d_done = sem("top_d_done")
        top_e_done = sem("top_e_done")
        x_hi_done = sem("x_hi_done")
        x_lo_done = sem("x_lo_done")
        w0_hi_done = sem("w0_hi_done")
        w0_lo_done = sem("w0_lo_done")
        act0_ready = sem("act0_ready")
        mul0_ready = sem("mul0_ready")
        silu_done = sem("silu_done")
        h0_done = sem("h0_done")
        h0_hi_done = sem("h0_hi_done")
        h0_lo_done = sem("h0_lo_done")
        out0_ready = sem("out0_ready")
        x1_done = sem("x1_done")
        x1_hi_done = sem("x1_hi_done")
        x1_lo_done = sem("x1_lo_done")
        w1_hi_done = sem("w1_hi_done")
        w1_split = [[sem(f"w1_{what}_split{k}") for what in ("gate_up", "down")] for k in range(MLPS)]
        act_ready = sem("act_ready")
        mul_ready = sem("mul_ready")
        gelu_done = sem("gelu_done")
        h_done = sem("h_done")
        h_hi_done = sem("h_hi_done")
        h_lo_done = sem("h_lo_done")
        down_done = sem("down_done")
        y_done = sem("y_done")
        stored = sem("stored")
        cond_loaded = sem("cond_loaded")

        def row(t, b):
            return t[:, bass.ds(b * S, S)]

        def chunk(t, c):
            return t[:, c * S:(c + 1) * S]

        block = ctx.enter_context(nc.Block())

        @block.sync
        def _(sp):
            sp.dma_start(cond_sb[:, :, :].rearrange("p b e -> p (b e)"),
                         cond.partition_broadcast(P)).then_inc(cond_loaded, 16)

            for b in range(B):
                r, loads_before = b % RING, b // RING
                sp.wait_ge(routed, b + 1)
                if loads_before:
                    sp.wait_ge(w0_loaded[r], 16 * loads_before)
                expert = sp.value_load(top_i[0:1, b * E:b * E + 1], min_val=0, max_val=E - 1)
                sp.dma_start(w0_raw[:, b * R0:(b + 1) * R0],
                             w0_packed[bass.ds(expert, 1), :, :].rearrange("e p n -> (e p) n")
                             ).then_inc(w0_loaded[r], 16)

            def load1(b, k):
                if b:
                    sp.wait_ge(w1_split[k][1], b)
                expert = sp.value_load(top_i[0:1, b * E + k:b * E + k + 1], min_val=0, max_val=E - 1)
                sp.dma_start(w1_raw[k][:, :],
                             w1_packed[bass.ds(expert, 1), :, :].rearrange("e p n -> (e p) n")
                             ).then_inc(w1_loaded[k], 16)

            def store(b):
                sp.wait_ge(y_done, b + 1)
                sp.dma_start(out_t[:, b * S:(b + 1) * S], row(x, b)).then_inc(stored, 16)

            for b in range(B):
                for k in range(TOP_K):
                    load1(b, k)
                if b == 0:
                    sp.dma_start(w1_raw[TOP_K][:, :], shared_packed).then_inc(w1_loaded[TOP_K], 16)
                if b >= 2:
                    store(b - 2)
            store(B - 2)
            store(B - 1)
            sp.wait_ge(stored, 16 * B)

        @block.gpsimd
        def _(pool):
            for b in range(B):
                r = b % W0_RING
                for n, (lo, hi) in enumerate(W0_PIECES):
                    pool.wait_ge(w0_hi_done, 2 * b + n + 1)
                    nc.gpsimd.tensor_tensor(w0_lo[r][:, lo:hi], w0_raw[:, b * R0 + lo:b * R0 + hi],
                                            w0_hi[r][:, lo:hi].bitcast(F32), ALU.subtract).then_inc(w0_lo_done, 1)

            def rest_w1(k, n, pieces):
                lo, hi = W1_PIECES[n]
                pool.wait_ge(w1_hi_done, pieces)
                nc.gpsimd.tensor_tensor(w1_lo[k][:, lo:hi], w1_raw[k][:, lo:hi], w1_hi[k][:, lo:hi].bitcast(F32),
                                        ALU.subtract).then_inc(w1_split[k][n], 1)

            for k in range(MLPS):
                for n in range(2):
                    rest_w1(k, n, 2 * k + n + 1)
            with pool.Fori(1, B) as b:
                for k in range(TOP_K):
                    for n in range(2):
                        rest_w1(k, n, b * (2 * TOP_K) + 2 + 2 * k + n + 1)

        @block.scalar
        def _(act):
            act.dma_start(x[:, 0:S], x_t[:, 0:S]).then_inc(x_loaded[0], 16)
            act.dma_start(x[:, S:], x_t[:, S:]).then_inc(x_loaded[1], 16)
            act.wait_ge(top_d_done, 1)
            nc.scalar.activation(top_e[:, :, :], top_d[:, :, :], ACT.Exp).then_inc(top_e_done, 1)
            def round_w0(b, n):
                r, (lo, hi) = b % W0_RING, W0_PIECES[n]
                act.wait_ge(w0_loaded[b % RING], 16 * (b // RING + 1))
                if b >= W0_RING:
                    act.wait_ge((mul0_ready, out0_ready)[n], b - W0_RING + 1)
                nc.scalar.copy(w0_hi[r][:, lo:hi], w0_raw[:, b * R0 + lo:b * R0 + hi]).then_inc(w0_hi_done, 1)

            def round_w1(b, k, n, first=False):
                lo, hi = W1_PIECES[n]
                if n == 0:
                    act.wait_ge(w1_loaded[k], b * 16 + 16)
                if not first:
                    act.wait_ge((mul_ready, down_done)[n], (b - 1) * STEPS + 2 * (k + 1))
                nc.scalar.copy(w1_hi[k][:, lo:hi], w1_raw[k][:, lo:hi]).then_inc(w1_hi_done, 1)

            def silu0(b):
                act.wait_ge(act0_ready, b + 1)
                for c in range(C0):
                    ins = nc.scalar.activation(chunk(act_h[b % RING], c), chunk(act_ps[b % RING], c), ACT.Silu,
                                               bias=w0_raw[:, b * R0 + BUP0 + c:b * R0 + BUP0 + c + 1])
                ins.then_inc(silu_done, 1)

            def round_h0(b):
                act.wait_ge(h0_done, b + 1)
                nc.scalar.copy(h_hi[b % RING][:, :], h[b % RING][:, :]).then_inc(h0_hi_done, 1)

            w1_first = [(k, n) for k in range(MLPS) for n in range(2)]
            act.wait_ge(x_loaded[0], 16)
            nc.scalar.copy(x_hi[:, 0:S], x[:, 0:S]).then_inc(x_hi_done, 1)
            for n in range(2):
                round_w0(0, n)
            act.wait_ge(x_loaded[1], 16)
            nc.scalar.copy(x_hi[:, S:], x[:, S:]).then_inc(x_hi_done, 1)
            for n in range(2):
                round_w0(1, n)
            silu0(0)
            round_w0(2, 0)
            for b in range(B):
                if b + 1 < B:
                    silu0(b + 1)
                round_h0(b)
                if b + 2 < B:
                    round_w0(b + 2, 1)
                if b + 3 < B:
                    round_w0(b + 3, 0)
                if b >= 4:
                    round_w1(0, *w1_first.pop(0), first=True)

            def gelu(n, r):
                act.wait_ge(act_ready, n + 1)
                nc.scalar.activation(act_h[r][:, :], act_ps[r][:, :], ACT.Gelu_apprx_tanh).then_inc(gelu_done, 1)

            def round_h(n, r):
                act.wait_ge(h_done, n + 1)
                nc.scalar.copy(h_hi[r][:, :], h[r][:, :]).then_inc(h_hi_done, 1)

            ahead = {2: (0, 0), 3: (0, 1), 4: (1, 0), 5: (1, 1)}

            def layer1(b, last=False):
                for s in range(STEPS):
                    if not (last and s == STEPS - 1):
                        gelu(b * STEPS + s + 1, (s + 1) % RING)
                    round_h(b * STEPS + s, s % RING)
                    if not last and s in ahead:
                        round_w1(b + 1, *ahead[s])

            gelu(0, 0)
            while w1_first:
                round_w1(0, *w1_first.pop(0), first=True)
            with act.Fori(0, B - 1) as b:
                layer1(b)
            layer1(B - 1, last=True)

        @block.vector
        def _(dve):
            dve.wait_ge(cond_loaded, 16)
            steps = [0]

            def step(ins):
                ins.then_inc(route_step, 1)
                steps[0] += 1
                dve.wait_ge(route_step, steps[0])

            for b in range(B):
                step(nc.vector.max(top_v[:, b, :], cond_sb[:, b, :]))
                nc.vector.max_index(top_i[:, b * E:(b + 1) * E], top_v[:, b, :], cond_sb[:, b, :]).then_inc(routed, 1)
            nc.vector.tensor_tensor(top_d[:, :, :], top_v[:, :, :], top_v[:, :, 0:1].to_broadcast([P, B, E]),
                                    ALU.subtract).then_inc(top_d_done, 1)
            dve.wait_ge(top_e_done, 1)
            step(nc.vector.reduce_sum(row_a[:, :], top_e[:, :, :], AXX))
            step(nc.vector.reciprocal(row_b[:, :], row_a[:, :]))
            step(nc.vector.tensor_tensor(rw[:, :, :], top_e[:, :, 0:TOP_K],
                                         row_b[:, :].unsqueeze(2).to_broadcast([P, B, TOP_K]), ALU.mult))
            step(nc.vector.reduce_sum(row_a[:, :], rw[:, :, :], AXX))
            step(nc.vector.reciprocal(row_b[:, :], row_a[:, :]))
            step(nc.vector.tensor_tensor(rw_n[:, :, :], rw[:, :, :],
                                         row_b[:, :].unsqueeze(2).to_broadcast([P, B, TOP_K]), ALU.mult))
            step(nc.vector.tensor_scalar(rw_t[:, :, :], rw_n[:, :, :], 1.0 - SCALE, None, ALU.mult))
            step(nc.vector.scalar_tensor_tensor(mix[:, :].rearrange("p (b k) -> p b k", k=TOP_K), rw_n[:, :, :],
                                                SCALE, rw_t[:, :, :], ALU.mult, ALU.add))

            for n, (lo, hi) in enumerate(((0, S), (S, B * S))):
                dve.wait_ge(x_hi_done, n + 1)
                nc.vector.tensor_tensor(x_lo[:, lo:hi], x[:, lo:hi], x_hi[:, lo:hi].bitcast(F32),
                                        ALU.subtract).then_inc(x_lo_done, 1)

            def product0(b):
                r = b % RING
                dve.wait_ge(mul0_ready, b + 1)
                dve.wait_ge(silu_done, b + 1)
                for c in range(C0):
                    at = b * R0 + BGATE0 + c
                    ins = nc.vector.scalar_tensor_tensor(chunk(h[r], c), chunk(mul_ps[r], c), w0_raw[:, at:at + 1],
                                                         chunk(act_h[r], c), ALU.add, ALU.mult)
                ins.then_inc(h0_done, 1)

            def rest_h0(b):
                r = b % RING
                dve.wait_ge(h0_hi_done, b + 1)
                nc.vector.tensor_tensor(h_lo[r][:, :], h[r][:, :], h_hi[r][:, :].bitcast(F32),
                                        ALU.subtract).then_inc(h0_lo_done, 1)

            def residual0(b):
                at = b * R0 + BDOWN0
                dve.wait_ge(out0_ready, b + 1)
                nc.vector.scalar_tensor_tensor(row(x1, b), out_ps[b % 2][:, 0:S], w0_raw[:, at:at + 1],
                                               row(x, b), ALU.add, ALU.add).then_inc(x1_done, 1)
                dve.wait_ge(x1_done, b + 1)
                nc.vector.tensor_copy(row(x1_hi, b), row(x1, b)).then_inc(x1_hi_done, 1)
                dve.wait_ge(x1_hi_done, b + 1)
                nc.vector.tensor_tensor(row(x1_lo, b), row(x1, b), row(x1_hi, b).bitcast(F32),
                                        ALU.subtract).then_inc(x1_lo_done, 1)

            product0(0)
            for b in range(B):
                if b + 1 < B:
                    product0(b + 1)
                rest_h0(b)
                if b:
                    residual0(b - 1)
            residual0(B - 1)

            def product(n, b, s):
                r, k = s % RING, s * HALF // C1
                dve.wait_ge(mul_ready, n + 1)
                dve.wait_ge(gelu_done, n + 1)
                if k < TOP_K:
                    ins = nc.vector.scalar_tensor_tensor(h[r][:, :], act_h[r][:, :],
                                                         mix[:, bass.ds(b * TOP_K + k, 1)],
                                                         mul_ps[r][:, :], ALU.mult, ALU.mult)
                else:
                    ins = nc.vector.tensor_tensor(h[r][:, :], act_h[r][:, :], mul_ps[r][:, :], ALU.mult)
                ins.then_inc(h_done, 1)

            def rest_h(n, r):
                dve.wait_ge(h_hi_done, n + 1)
                nc.vector.tensor_tensor(h_lo[r][:, :], h[r][:, :], h_hi[r][:, :].bitcast(F32),
                                        ALU.subtract).then_inc(h_lo_done, 1)

            def residual1(b):
                dve.wait_ge(down_done, (b + 1) * STEPS)
                nc.vector.tensor_tensor(row(x, b), out_ps[0][:, 0:S], row(x1, b), ALU.add).then_inc(y_done, 1)

            def layer1(b, first=False, last=False):
                for s in range(STEPS):
                    if s == 1 and not first:
                        residual1(b - 1)
                    if s < STEPS - 1:
                        product(b * STEPS + s + 1, b, s + 1)
                    elif not last:
                        product((b + 1) * STEPS, b + 1, 0)
                    rest_h(b * STEPS + s, s % RING)

            product(0, 0, 0)
            layer1(0, first=True)
            with dve.Fori(1, B - 1) as b:
                layer1(b)
            layer1(B - 1, last=True)
            residual1(B - 1)

        @block.tensor
        def _(pe):
            def product3(out, w_hi, w_lo, m_hi, m_lo, start, stop):
                nc.tensor.matmul(out, w_hi, m_hi, start=start, stop=False)
                nc.tensor.matmul(out, w_hi, m_lo, start=False, stop=False)
                return nc.tensor.matmul(out, w_lo, m_hi, start=False, stop=stop)

            def up0(b):
                r, w = b % RING, b % W0_RING
                pe.wait_ge(w0_lo_done, 2 * b + 1)
                for ps_t, at, ready in ((act_ps, UP0, act0_ready), (mul_ps, GATE0, mul0_ready)):
                    for c in range(C0):
                        cols = slice(at + c * P, at + (c + 1) * P)
                        last = product3(chunk(ps_t[r], c), w0_hi[w][:, cols], w0_lo[w][:, cols],
                                        row(x_hi, b), row(x_lo, b), True, True)
                    last.then_inc(ready, 1)

            def down0(b):
                r, w = b % RING, b % W0_RING
                pe.wait_ge(w0_lo_done, 2 * b + 2)
                pe.wait_ge(h0_lo_done, b + 1)
                if b >= 2:
                    pe.wait_ge(x1_done, b - 1)
                for c in range(C0):
                    cols = slice(DOWN0 + c * D, DOWN0 + (c + 1) * D)
                    last = product3(out_ps[b % 2][:, 0:S], w0_hi[w][:, cols], w0_lo[w][:, cols],
                                    chunk(h_hi[r], c), chunk(h_lo[r], c), c == 0, c == C0 - 1)
                last.then_inc(out0_ready, 1)

            pe.wait_ge(x_lo_done, 1)
            up0(0)
            pe.wait_ge(x_lo_done, 2)
            for b in range(1, LAG):
                up0(b)
            for b in range(B):
                if b + LAG < B:
                    up0(b + LAG)
                down0(b)

            def up1(n, b, s, first=False):
                r, k, half = s % RING, s * HALF // C1, s % (C1 // HALF)
                if s == 0:
                    pe.wait_ge(x1_lo_done, b + 1)
                if half == 0:
                    pe.wait_ge(w1_split[k][0], b + 1 if k < TOP_K else 1)
                if not first:
                    pe.wait_ge(gelu_done, n - RING + 1)
                    pe.wait_ge(h_done, n - RING + 1)
                for ps_t, at, ready in ((act_ps, GATE1, act_ready), (mul_ps, UP1, mul_ready)):
                    for c in range(HALF):
                        lo = at + (half * HALF + c) * P
                        last = product3(chunk(ps_t[r], c), w1_hi[k][:, lo:lo + P], w1_lo[k][:, lo:lo + P],
                                        row(x1_hi, b), row(x1_lo, b), True, True)
                    last.then_inc(ready, 1)

            def down1(n, b, s):
                r, k, half = s % RING, s * HALF // C1, s % (C1 // HALF)
                if s == 0:
                    pe.wait_ge(y_done, b)
                if half == 0:
                    pe.wait_ge(w1_split[k][1], b + 1 if k < TOP_K else 1)
                pe.wait_ge(h_lo_done, n + 1)
                for c in range(HALF):
                    lo = DOWN1 + (half * HALF + c) * D
                    last = product3(out_ps[0][:, 0:S], w1_hi[k][:, lo:lo + D], w1_lo[k][:, lo:lo + D],
                                    chunk(h_hi[r], c), chunk(h_lo[r], c),
                                    s == 0 and c == 0, s == STEPS - 1 and c == HALF - 1)
                last.then_inc(down_done, 1)

            def layer1(b, first=False, last=False):
                for s in range(STEPS):
                    ahead = s + LAG
                    if ahead < STEPS:
                        up1(b * STEPS + ahead, b, ahead, first=first and ahead < RING)
                    elif not last:
                        up1((b + 1) * STEPS + ahead - STEPS, b + 1, ahead - STEPS)
                    down1(b * STEPS + s, b, s)

            for s in range(LAG):
                up1(s, 0, s, first=True)
            layer1(0, first=True)
            with pe.Fori(1, B - 1) as b:
                layer1(b)
            layer1(B - 1, last=True)


def kernel(x, cond_8, L0_cond_W_up, L0_cond_b_up, L0_cond_W_gate, L0_cond_b_gate, L0_cond_W_down, L0_cond_b_down,
           L1_cond_skill_gate, L1_cond_skill_up, L1_cond_skill_down,
           L1_cond_shared_gate, L1_cond_shared_up, L1_cond_shared_down):
    import numpy as np
    import concourse.bacc as bacc
    from concourse.bass_utils import run_bass_kernel_spmd

    def chunks_to_columns(w, parts):
        *lead, rows, n = w.shape
        w = w.reshape(*lead, parts, rows // parts, n)
        return np.moveaxis(w, -3, -2).reshape(*lead, rows // parts, parts * n)

    x_t = np.ascontiguousarray(np.asarray(x).reshape(B * S, D).T)
    cond = np.ascontiguousarray(np.asarray(cond_8).reshape(B * E))
    w0 = np.concatenate([
        np.swapaxes(np.asarray(L0_cond_W_up), 1, 2),
        np.swapaxes(np.asarray(L0_cond_W_gate), 1, 2),
        chunks_to_columns(np.swapaxes(np.asarray(L0_cond_W_down), 1, 2), C0),
        chunks_to_columns(np.asarray(L0_cond_b_up)[:, :, None], C0),
        chunks_to_columns(np.asarray(L0_cond_b_gate)[:, :, None], C0),
        np.asarray(L0_cond_b_down)[:, :, None],
    ], axis=-1)
    w1 = np.concatenate([np.asarray(L1_cond_skill_gate), np.asarray(L1_cond_skill_up),
                         chunks_to_columns(np.asarray(L1_cond_skill_down), C1)], axis=-1)
    shared = np.concatenate([np.asarray(L1_cond_shared_gate), np.asarray(L1_cond_shared_up),
                             chunks_to_columns(np.asarray(L1_cond_shared_down), C1)], axis=-1)
    arrays = {"x_t": x_t, "cond": cond, "w0": w0, "w1": w1, "shared": shared}
    arrays = {name: np.ascontiguousarray(a) for name, a in arrays.items()}

    nc = bacc.Bacc("TRN2", target_bir_lowering=False, num_devices=1)
    ins = [nc.dram_tensor(name, a.shape, mybir.dt.from_np(a.dtype), kind="ExternalInput").ap()
           for name, a in arrays.items()]
    out = nc.dram_tensor("out_t", (D, B * S), F32, kind="ExternalOutput").ap()
    program(nc, *ins, out)
    got = run_bass_kernel_spmd(nc, [arrays], core_ids=[0]).results[0]["out_t"]
    return np.ascontiguousarray(got.T).reshape(B, S, D)
```

```python
from contextlib import ExitStack

import concourse.bass as bass
from concourse import mybir

F32 = mybir.dt.float32
F32R = mybir.dt.float32r
U32 = mybir.dt.uint32
ALU = mybir.AluOpType
ACT = mybir.ActivationFunctionType
AXX = mybir.AxisListType.X

B, S, D = 8, 256, 128
E, TOP_K = 8, 2
H0, H1 = 256, 512
P = 128
C0, C1 = H0 // P, H1 // P
SCALE = 1.0 / 12

UP0, GATE0 = 0, H0
BIAS0 = 2 * H0
DOWN0 = BIAS0 + 2 * C0 + 1
W0 = DOWN0 + C0 * D
HALF = 2
DOWN1 = 2 * H1
W1 = DOWN1 + C1 * D
W0_PIECES = ((0, BIAS0), (DOWN0, W0))
W1_PIECES = ((0, DOWN1), (DOWN1, W1))
SHARED_PIECES = ((0, DOWN1 // 2), (DOWN1 // 2, DOWN1), (DOWN1, W1))

MLPS = TOP_K + 1
STEPS = MLPS * C1 // HALF
H_RING = 3
PS_RING = 2
LAG = 2
AHEAD = 2
assert (B - AHEAD) % 2 == 0
LOOP_END = 1 + (B - AHEAD - 1) // 2 * 2
assert STEPS % H_RING == 0 and STEPS % PS_RING == 0
UP_AT, TANH_AT, SIGMOID_AT, SILU_AT, PRODUCT_AT, ROUND_AT, REST_AT, DOWN_AT = 1, 2, 2, 3, 4, 5, 5, 5
RESIDUAL_AT, X_HI_AT, X_LO_AT = 0, 1, 2
BIAS_AT = 1
W0_AT = {0: 0, 2: 1}
W1_AT = {0: (2, 1, 0), 3: (1, 0, 1), 4: (2, 0, 1), 5: (1, 1, 1)}
EARLY_X = AHEAD + 1
assert B - 1 - EARLY_X == STEPS - 2


def program(nc, x_t, cond, w0_packed, w1_packed, shared_packed, out_t):
    ctx = ExitStack()
    with ctx:
        def sb(name, shape, dt=F32):
            return ctx.enter_context(nc.sbuf_tensor(name, shape, dt))

        def ps(name):
            return ctx.enter_context(nc.psum_tensor(name, [P, 512], F32))

        def sem(name):
            return ctx.enter_context(nc.semaphore(name))

        cond_sb = sb("cond_sb", [P, B, E])
        top_v = sb("top_v", [P, B, E])
        top_i = sb("top_i", [P, B * E], U32)
        top_d = sb("top_d", [P, B, E])
        top_e = sb("top_e", [P, B, E])
        row_a = sb("row_a", [P, B])
        row_b = sb("row_b", [P, B])
        rw = sb("rw", [P, B, TOP_K])
        rw_n = sb("rw_n", [P, B, TOP_K])
        rw_t = sb("rw_t", [P, B, TOP_K])
        mix = sb("mix", [P, B * TOP_K])

        x = sb("x", [P, B * S])
        x_hi = sb("x_hi", [P, B * S], F32R)
        x_lo = sb("x_lo", [P, B * S], F32R)
        x1 = sb("x1", [P, B * S])
        x1_hi = sb("x1_hi", [P, B * S], F32R)
        x1_lo = sb("x1_lo", [P, B * S], F32R)

        w0_raw = [sb(f"w0_raw{j}", [P, W0]) for j in range(2)]
        w0_hi = [sb(f"w0_hi{j}", [P, W0], F32R) for j in range(2)]
        w0_lo = [sb(f"w0_lo{j}", [P, W0], F32R) for j in range(2)]
        bias0 = [sb(f"bias0_{j}", [P, DOWN0 - BIAS0]) for j in range(2)]
        half_bup0 = [sb(f"half_bup0_{j}", [P, C0]) for j in range(2)]
        w1_raw = [[sb(f"w1_raw{k}_{j}", [P, W1]) for j in range(2 if k else 1)] for k in range(MLPS)]
        w1_hi = [sb(f"w1_hi{k}", [P, W1], F32R) for k in range(MLPS)]
        w1_lo = [sb(f"w1_lo{k}", [P, W1], F32R) for k in range(MLPS)]

        tanh0 = sb("tanh0", [P, C0 * S])
        sigmoid0 = sb("sigmoid0", [P, C0 * S])
        silu0 = [sb(f"silu0_{j}", [P, C0 * S]) for j in range(2)]
        h0 = [sb(f"h0_{j}", [P, C0 * S]) for j in range(2)]
        h0_hi = sb("h0_hi", [P, C0 * S], F32R)
        h0_lo = sb("h0_lo", [P, C0 * S], F32R)
        gelu_h = [sb(f"gelu_h1_{r}", [P, HALF * S]) for r in range(H_RING)]
        h = [sb(f"h1_{r}", [P, HALF * S]) for r in range(H_RING)]
        h_hi = [sb(f"h1_hi{r}", [P, HALF * S], F32R) for r in range(H_RING)]
        h_lo = [sb(f"h1_lo{r}", [P, HALF * S], F32R) for r in range(H_RING)]

        zeros_w = sb("zeros_w", [P, P], F32R)
        zeros_m = sb("zeros_m", [P, 512], F32R)
        table_in = sb("table_in", [P, 1])
        table_out = sb("table_out", [P, 2])

        gate1_ps = [ps(f"gate1_ps{r}") for r in range(PS_RING)]
        up1_ps = [ps(f"up1_ps{r}") for r in range(PS_RING)]
        out1_ps = ps("out1_ps")
        up0_ps, gate0_ps, out0_ps = ps("up0_ps"), ps("gate0_ps"), ps("out0_ps")

        def slot0(b):
            return int(isinstance(b, int) and b == 1)

        def loaded(b, odd):
            return (b - odd) * 8 + 16

        def banks0(b):
            return (gate1_ps[1], up1_ps[1]) if slot0(b) else (up0_ps, gate0_ps)

        def split(parts):
            width = HALF * S // parts
            return [slice(i * width, (i + 1) * width) for i in range(parts)]

        x_loaded = [sem(f"x_loaded{n}") for n in range(2)]
        w0_loaded = [sem(f"w0_loaded{j}") for j in range(2)]
        down0_loaded = [sem(f"down0_loaded{b}") for b in range(AHEAD)]
        shared_loaded = [sem(f"shared_loaded{n}") for n in range(len(SHARED_PIECES))]
        w1_loaded = [[sem(f"w1_loaded{k}_{j}") for j in range(2)] if k else None for k in range(MLPS)]
        routed = sem("routed")
        route_step = sem("route_step")
        top_d_done = sem("top_d_done")
        top_e_done = sem("top_e_done")
        zeroed = sem("zeroed")
        x_hi_done = sem("x_hi_done")
        x_lo_first = sem("x_lo_first")
        x_lo_done = sem("x_lo_done")
        up_gate0_hi_first = sem("up_gate0_hi_first")
        up_gate0_lo_first = sem("up_gate0_lo_first")
        down0_lo_first = sem("down0_lo_first")
        w0_hi_done = sem("w0_hi_done")
        w0_lo_done = sem("w0_lo_done")
        bias0_ready = sem("bias0_ready")
        up0_ready = sem("up0_ready")
        gate0_ready = sem("gate0_ready")
        silu0_first = sem("silu0_first")
        tanh0_done = sem("tanh0_done")
        silu0_step = sem("silu0_step")
        h0_done = sem("h0_done")
        h0_hi_done = sem("h0_hi_done")
        h0_lo_done = sem("h0_lo_done")
        out0_ready = sem("out0_ready")
        x1_done = sem("x1_done")
        x1_hi_done = sem("x1_hi_done")
        x1_lo_done = sem("x1_lo_done")
        shared_hi_done = [sem(f"shared_hi_done{n}") for n in range(len(SHARED_PIECES))]
        w1_hi_done = sem("w1_hi_done")
        w1_split = [[sem(f"w1_{what}_split{k}") for what in ("gate_up", "down")] for k in range(MLPS)]
        gate1_ready = sem("gate1_ready")
        up1_ready = sem("up1_ready")
        gelu_done = sem("gelu_done")
        h_done = sem("h_done")
        h_hi_done = sem("h_hi_done")
        h_lo_done = sem("h_lo_done")
        down_done = sem("down_done")
        y_done = sem("y_done")
        stored = sem("stored")
        cond_loaded = sem("cond_loaded")

        def row(t, b):
            return t[:, bass.ds(b * S, S)]

        def chunk(t, c):
            return t[:, c * S:(c + 1) * S]

        block = ctx.enter_context(nc.Block())

        @block.sync
        def _(sp):
            sp.dma_start(cond_sb[:, :, :].rearrange("p b e -> p (b e)"),
                         cond.partition_broadcast(P)).then_inc(cond_loaded, 16)

            def load_shared(n):
                lo, hi = SHARED_PIECES[n]
                sp.dma_start(w1_raw[0][0][:, lo:hi], shared_packed[:, lo:hi]).then_inc(shared_loaded[n], 16)

            for n in range(2):
                load_shared(n)

            def load0(b):
                sp.wait_ge(routed, b + 1)
                if b >= 2 * AHEAD:
                    sp.wait_ge(w0_lo_done, 2 * (b - 2 * AHEAD + 1))
                elif b >= AHEAD:
                    sp.wait_ge(up_gate0_lo_first, b - AHEAD + 1)
                    sp.wait_ge(down0_lo_first, b - AHEAD + 1)
                if b >= AHEAD:
                    sp.wait_ge(bias0_ready, 2 * (b - AHEAD + 1))
                expert = sp.value_load(top_i[0:1, b * E:b * E + 1], min_val=0, max_val=E - 1)
                raw, w = w0_raw[b % 2], w0_packed[bass.ds(expert, 1), :, :].rearrange("e p n -> (e p) n")
                if b >= AHEAD:
                    sp.dma_start(raw[:, :], w).then_inc(w0_loaded[b % 2], 16)
                    return None
                sp.dma_start(raw[:, 0:DOWN0], w[:, 0:DOWN0]).then_inc(w0_loaded[b], 16)
                return raw[:, DOWN0:W0], w[:, DOWN0:W0]

            def load1(b, k):
                sp.wait_ge(routed, b + 1)
                if b >= 2:
                    sp.wait_ge(w1_split[k][1], b - 1)
                expert = sp.value_load(top_i[0:1, b * E + k - 1:b * E + k], min_val=0, max_val=E - 1)
                sp.dma_start(w1_raw[k][b % 2][:, :],
                             w1_packed[bass.ds(expert, 1), :, :].rearrange("e p n -> (e p) n")
                             ).then_inc(w1_loaded[k][b % 2], 16)

            def store(b):
                sp.wait_ge(y_done, b + 1)
                sp.dma_start(out_t[:, b * S:(b + 1) * S], row(x, b)).then_inc(stored, 16)

            downs = [load0(b) for b in range(AHEAD)]
            for (raw, w), loaded0 in zip(downs, down0_loaded):
                sp.dma_start(raw, w).then_inc(loaded0, 16)
            load1(0, 1)
            load_shared(2)
            load0(AHEAD)
            load1(0, 2)
            sp.dma_start(x[:, EARLY_X * S:B * S], x_t[:, EARLY_X * S:B * S]).then_inc(x_loaded[1], 16)
            load1(1, 1)
            load0(AHEAD + 1)
            load1(1, 2)
            for b in range(B):
                if b + 2 < B:
                    load1(b + 2, 1)
                if b:
                    store(b - 1)
                if b + 2 < B:
                    load1(b + 2, 2)
                if b + 2 + AHEAD < B:
                    load0(b + 2 + AHEAD)
            store(B - 1)
            sp.wait_ge(stored, 16 * B)

        @block.gpsimd
        def _(pool):
            def rest_w0(n, pieces, odd):
                lo, hi = W0_PIECES[n]
                pool.wait_ge(w0_hi_done, pieces)
                nc.gpsimd.tensor_tensor(w0_lo[0][:, lo:hi], w0_raw[odd][:, lo:hi], w0_hi[0][:, lo:hi].bitcast(F32),
                                        ALU.subtract).then_inc(w0_lo_done, 1)

            def rest_down0_first(b):
                lo, hi = W0_PIECES[1]
                pool.wait_ge(w0_hi_done, b + 1)
                nc.gpsimd.tensor_tensor(w0_lo[b][:, lo:hi], w0_raw[b][:, lo:hi], w0_hi[b][:, lo:hi].bitcast(F32),
                                        ALU.subtract).then_inc(down0_lo_first, 1)

            def rest_shared(n):
                lo, hi = SHARED_PIECES[n]
                pool.wait_ge(shared_hi_done[n], 1)
                nc.gpsimd.tensor_tensor(w1_lo[0][:, lo:hi], w1_raw[0][0][:, lo:hi], w1_hi[0][:, lo:hi].bitcast(F32),
                                        ALU.subtract).then_inc(w1_split[0][n // 2], 1)

            def rest_w1(k, n, pieces, odd):
                lo, hi = W1_PIECES[n]
                pool.wait_ge(w1_hi_done, pieces)
                nc.gpsimd.tensor_tensor(w1_lo[k][:, lo:hi], w1_raw[k][odd][:, lo:hi], w1_hi[k][:, lo:hi].bitcast(F32),
                                        ALU.subtract).then_inc(w1_split[k][n], 1)

            def rest_x(b):
                pool.wait_ge(x_hi_done, b - EARLY_X + 2)
                nc.gpsimd.tensor_tensor(row(x_lo, b), row(x, b), row(x_hi, b).bitcast(F32),
                                        ALU.subtract).then_inc(x_lo_done, 1)

            def layer1(b, odd, first=False, with0=True, last=False, last_x=False):
                pieces = b * len(W1_AT) + len(W1_AT)
                for s in range(STEPS):
                    if first and s == 1:
                        rest_w1(*W1_AT[0][:2], pieces, 0)
                    elif s in W1_AT and not (first and s == 0):
                        k, n, ahead = W1_AT[s]
                        if not ahead or not last:
                            rest_w1(k, n, pieces + sorted(W1_AT).index(s), (odd + ahead) % 2)
                    if s in W0_AT and with0 and not (first and s == 0):
                        rest_w0(W0_AT[s], b * 2 + AHEAD + W0_AT[s] + 1, odd)
                    if first and 0 < s < STEPS - 1:
                        rest_x(EARLY_X + s - 1)
                    if last_x and s == 0:
                        rest_x(B - 1)

            rest_shared(0)
            rest_down0_first(0)
            rest_down0_first(1)
            rest_shared(1)
            rest_w1(1, 0, 1, 0)
            rest_shared(2)
            rest_w1(1, 1, 2, 0)
            rest_w0(0, AHEAD + 1, 0)
            rest_w1(2, 0, 3, 0)
            layer1(0, 0, first=True)
            with pool.Fori(1, LOOP_END, 2) as b:
                layer1(b, 1)
                layer1(b + 1, 0)
            for b in range(LOOP_END, B):
                layer1(b, b % 2, with0=b + AHEAD < B, last=b == B - 1, last_x=b + AHEAD == B - 1)

        @block.scalar
        def _(act):
            act.dma_start(x[:, 0:EARLY_X * S], x_t[:, 0:EARLY_X * S]).then_inc(x_loaded[0], 16)
            act.wait_ge(x_loaded[0], 16)
            nc.scalar.copy(x_hi[:, 0:EARLY_X * S], x[:, 0:EARLY_X * S]).then_inc(x_hi_done, 1)
            act.wait_ge(top_d_done, 1)
            nc.scalar.activation(top_e[:, :, :], top_d[:, :, :], ACT.Exp).then_inc(top_e_done, 1)
            act.wait_ge(zeroed, 1)
            nc.scalar.activation(table_out[:, 0:1], table_in[:, :], ACT.Silu)

            def round_x(b):
                if b == EARLY_X:
                    act.wait_ge(x_loaded[1], 16)
                nc.scalar.copy(row(x_hi, b), row(x, b)).then_inc(x_hi_done, 1)

            def round_w0(b, odd, n):
                j, (lo, hi) = slot0(b), W0_PIECES[n]
                if n == 0:
                    act.wait_ge(w0_loaded[odd], loaded(b, odd))
                elif isinstance(b, int) and b < AHEAD:
                    act.wait_ge(down0_loaded[b], 16)
                if not isinstance(b, int) or b >= AHEAD:
                    act.wait_ge((gate0_ready, out0_ready)[n], b)
                nc.scalar.copy(w0_hi[j][:, lo:hi], w0_raw[odd][:, lo:hi]).then_inc(w0_hi_done, 1)

            def round_w1(b, odd, k, n, first=False):
                lo, hi = W1_PIECES[n]
                if n == 0:
                    act.wait_ge(w1_loaded[k][odd], loaded(b, odd))
                if not first:
                    act.wait_ge((up1_ready, down_done)[n], (b - 1) * STEPS + 2 * (k + 1))
                nc.scalar.copy(w1_hi[k][:, lo:hi], w1_raw[k][odd][:, lo:hi]).then_inc(w1_hi_done, 1)

            def silu(b):
                j, (up_ps, _) = slot0(b), banks0(b)
                act.wait_ge(bias0_ready, (b + 1) * 2)
                act.wait_ge(up0_ready, b + 1)
                for c in range(C0):
                    nc.scalar.activation(chunk(silu0[j], c), chunk(up_ps, c), ACT.Silu,
                                         bias=bias0[j][:, c:c + 1]).then_inc(silu0_first, 1)

            def half_tanh(b):
                j, (up_ps, _) = slot0(b), banks0(b)
                act.wait_ge(bias0_ready, (b + 1) * 2)
                act.wait_ge(up0_ready, b + 1)
                for c in range(C0):
                    ins = nc.scalar.activation(chunk(tanh0, c), chunk(up_ps, c), ACT.Tanh,
                                               bias=half_bup0[j][:, c:c + 1], scale=0.5)
                ins.then_inc(tanh0_done, 1)

            def round_h0(b):
                act.wait_ge(h0_done, (b + 1) * C0)
                act.wait_ge(out0_ready, b)
                nc.scalar.copy(h0_hi[:, :], h0[0][:, :]).then_inc(h0_hi_done, C0)

            def round_h0_first(b):
                if b:
                    act.wait_ge(out0_ready, b)
                for c in range(C0):
                    act.wait_ge(h0_done, b * C0 + c + 1)
                    nc.scalar.copy(chunk(h0_hi, c), chunk(h0[slot0(b)], c)).then_inc(h0_hi_done, 1)

            def gelu(n, s, parts=1):
                act.wait_ge(gate1_ready, n + 1)
                for cols in split(parts):
                    nc.scalar.activation(gelu_h[s % H_RING][:, cols], gate1_ps[s % PS_RING][:, cols],
                                         ACT.Gelu_apprx_tanh).then_inc(gelu_done, 1)

            def round_h(n, s, parts=1):
                for i, cols in enumerate(split(parts)):
                    act.wait_ge(h_done, n + 1 + i)
                    nc.scalar.copy(h_hi[s % H_RING][:, cols], h[s % H_RING][:, cols]).then_inc(h_hi_done, 1)

            def layer1(b, odd, first=False, with0=True, last=False, last_x=False):
                for s in range(STEPS):
                    if last and s == STEPS - 2:
                        round_h(b * STEPS + s, s)
                        gelu(b * STEPS + s + 1, s + 1, HALF)
                    elif last and s == STEPS - 1:
                        round_h(b * STEPS + s, s, HALF)
                    else:
                        gelu(b * STEPS + s + 1, (s + 1) % STEPS)
                        round_h(b * STEPS + s, s)
                    if first and s == 0:
                        round_w0(AHEAD, 0, 0)
                    if s == ROUND_AT and with0:
                        round_h0(b + AHEAD)
                    if first and s == 1:
                        for n in range(2):
                            round_w1(0, 0, 2, n, first=True)
                    elif s in W1_AT and not (first and s == 0):
                        k, n, ahead = W1_AT[s]
                        if not ahead or not last:
                            round_w1(b + ahead, (odd + ahead) % 2, k, n)
                    if s in W0_AT and with0 and not (first and s == 0):
                        round_w0(b + AHEAD, odd, W0_AT[s])
                    if s == TANH_AT and with0:
                        half_tanh(b + AHEAD)
                    if first and 0 < s < STEPS - 1:
                        round_x(EARLY_X + s - 1)
                    if last_x and s == 0:
                        round_x(B - 1)

            def round_shared(n):
                lo, hi = SHARED_PIECES[n]
                act.wait_ge(shared_loaded[n], 16)
                nc.scalar.copy(w1_hi[0][:, lo:hi], w1_raw[0][0][:, lo:hi]).then_inc(shared_hi_done[n], 1)

            for n in range(2):
                round_shared(n)
            for b in range(AHEAD):
                round_w0(b, b % 2, 1)
            silu(0)
            round_h0_first(0)
            silu(1)
            round_w1(0, 0, 1, 0, first=True)
            nc.scalar.activation(table_out[:, 1:2], table_in[:, :], ACT.Gelu_apprx_tanh)
            gelu(0, 0)
            round_h0_first(1)
            round_w1(0, 0, 1, 1, first=True)
            layer1(0, 0, first=True)
            with act.Fori(1, LOOP_END, 2) as b:
                layer1(b, 1)
                layer1(b + 1, 0)
            for b in range(LOOP_END, B):
                layer1(b, b % 2, with0=b + AHEAD < B, last=b == B - 1, last_x=b + AHEAD == B - 1)

        @block.vector
        def _(dve):
            nc.vector.memset(table_in[:, :], 0.0)
            nc.vector.memset(zeros_w[:, :].bitcast(F32), 0.0)
            nc.vector.memset(zeros_m[:, :].bitcast(F32), 0.0).then_inc(zeroed, 1)
            dve.wait_ge(cond_loaded, 16)
            steps = [0]

            def step(ins):
                ins.then_inc(route_step, 1)
                steps[0] += 1
                dve.wait_ge(route_step, steps[0])

            for b in range(B):
                step(nc.vector.max(top_v[:, b, :], cond_sb[:, b, :]))
                nc.vector.max_index(top_i[:, b * E:(b + 1) * E], top_v[:, b, :], cond_sb[:, b, :]).then_inc(routed, 1)
            nc.vector.tensor_tensor(top_d[:, :, :], top_v[:, :, :], top_v[:, :, 0:1].to_broadcast([P, B, E]),
                                    ALU.subtract).then_inc(top_d_done, 1)

            dve.wait_ge(x_hi_done, 1)
            nc.vector.tensor_tensor(x_lo[:, 0:EARLY_X * S], x[:, 0:EARLY_X * S], x_hi[:, 0:EARLY_X * S].bitcast(F32),
                                    ALU.subtract).then_inc(x_lo_first, 1)

            def round_shared(n):
                lo, hi = SHARED_PIECES[n]
                dve.wait_ge(shared_loaded[n], 16)
                nc.vector.tensor_copy(w1_hi[0][:, lo:hi], w1_raw[0][0][:, lo:hi]).then_inc(shared_hi_done[n], 1)

            def softmax_sum():
                dve.wait_ge(top_e_done, 1)
                step(nc.vector.reduce_sum(row_a[:, :], top_e[:, :, :], AXX))
                step(nc.vector.reciprocal(row_b[:, :], row_a[:, :]))

            def probabilities():
                step(nc.vector.tensor_tensor(rw[:, :, :], top_e[:, :, 0:TOP_K],
                                             row_b[:, :].unsqueeze(2).to_broadcast([P, B, TOP_K]), ALU.mult))
                step(nc.vector.reduce_sum(row_a[:, :], rw[:, :, :], AXX))
                step(nc.vector.reciprocal(row_b[:, :], row_a[:, :]))

            def weigh():
                step(nc.vector.tensor_tensor(rw_n[:, :, :], rw[:, :, :],
                                             row_b[:, :].unsqueeze(2).to_broadcast([P, B, TOP_K]), ALU.mult))
                step(nc.vector.tensor_scalar(rw_t[:, :, :], rw_n[:, :, :], 1.0 - SCALE, None, ALU.mult))
                step(nc.vector.scalar_tensor_tensor(mix[:, :].rearrange("p (b k) -> p b k", k=TOP_K), rw_n[:, :, :],
                                                    SCALE, rw_t[:, :, :], ALU.mult, ALU.add))

            def split_up_gate0(b):
                lo, hi = W0_PIECES[0]
                dve.wait_ge(w0_loaded[b], 16)
                nc.vector.tensor_copy(w0_hi[b][:, lo:hi], w0_raw[b][:, lo:hi]).then_inc(up_gate0_hi_first, 1)
                dve.wait_ge(up_gate0_hi_first, b + 1)
                nc.vector.tensor_tensor(w0_lo[b][:, lo:hi], w0_raw[b][:, lo:hi],
                                        w0_hi[b][:, lo:hi].bitcast(F32), ALU.subtract
                                        ).then_inc(up_gate0_lo_first, 1)

            def copy_bias(b, odd):
                j = slot0(b)
                dve.wait_ge(w0_loaded[odd], loaded(b, odd))
                nc.vector.tensor_copy(bias0[j][:, :], w0_raw[odd][:, BIAS0:DOWN0]).then_inc(bias0_ready, 1)
                nc.vector.tensor_scalar(half_bup0[j][:, :], w0_raw[odd][:, BIAS0:BIAS0 + C0], 0.5, None,
                                        ALU.mult).then_inc(bias0_ready, 1)

            def sigmoid(b):
                dve.wait_ge(tanh0_done, b - AHEAD + 1)
                nc.vector.tensor_scalar(sigmoid0[:, :], tanh0[:, :], 0.5, 0.5, ALU.mult, ALU.add
                                        ).then_inc(silu0_step, 1)

            def silu(b):
                j, (up_ps, _) = slot0(b), banks0(b)
                dve.wait_ge(silu0_step, (b - AHEAD) * 2 + 1)
                for c in range(C0):
                    ins = nc.vector.scalar_tensor_tensor(chunk(silu0[0], c), chunk(up_ps, c), bias0[j][:, c:c + 1],
                                                         chunk(sigmoid0, c), ALU.add, ALU.mult)
                ins.then_inc(silu0_step, 1)

            def product0(b):
                j, (_, gate_ps) = slot0(b), banks0(b)
                dve.wait_ge(gate0_ready, b + 1)
                for c in range(C0):
                    if isinstance(b, int) and b < AHEAD:
                        dve.wait_ge(silu0_first, b * C0 + c + 1)
                    elif c == 0:
                        dve.wait_ge(silu0_step, (b - AHEAD) * 2 + 2)
                    nc.vector.scalar_tensor_tensor(chunk(h0[slot0(b)], c), chunk(gate_ps, c),
                                                   bias0[j][:, C0 + c:C0 + c + 1],
                                                   chunk(silu0[j], c), ALU.add, ALU.mult).then_inc(h0_done, 1)

            def rest_h0(b):
                dve.wait_ge(h0_hi_done, (b + 1) * C0)
                nc.vector.tensor_tensor(h0_lo[:, :], h0[0][:, :], h0_hi[:, :].bitcast(F32),
                                        ALU.subtract).then_inc(h0_lo_done, C0)

            def rest_h0_first(b):
                for c in range(C0):
                    dve.wait_ge(h0_hi_done, b * C0 + c + 1)
                    nc.vector.tensor_tensor(chunk(h0_lo, c), chunk(h0[slot0(b)], c), chunk(h0_hi, c).bitcast(F32),
                                            ALU.subtract).then_inc(h0_lo_done, 1)

            def residual0(b):
                dve.wait_ge(out0_ready, b + 1)
                nc.vector.scalar_tensor_tensor(row(x1, b), out0_ps[:, 0:S], bias0[slot0(b)][:, 2 * C0:2 * C0 + 1],
                                               row(x, b), ALU.add, ALU.add).then_inc(x1_done, 1)

            def round_x1(b):
                dve.wait_ge(x1_done, b + 1)
                nc.vector.tensor_copy(row(x1_hi, b), row(x1, b)).then_inc(x1_hi_done, 1)

            def rest_x1(b):
                dve.wait_ge(x1_hi_done, b + 1)
                nc.vector.tensor_tensor(row(x1_lo, b), row(x1, b), row(x1_hi, b).bitcast(F32),
                                        ALU.subtract).then_inc(x1_lo_done, 1)

            def product(n, b, s, parts=1):
                r, k = s % H_RING, s * HALF // C1
                dve.wait_ge(up1_ready, n + 1)
                for i, cols in enumerate(split(parts)):
                    dve.wait_ge(gelu_done, n + 1 + i)
                    up = up1_ps[s % PS_RING][:, cols]
                    if k:
                        ins = nc.vector.scalar_tensor_tensor(h[r][:, cols], gelu_h[r][:, cols],
                                                             mix[:, bass.ds(b * TOP_K + k - 1, 1)], up,
                                                             ALU.mult, ALU.mult)
                    else:
                        ins = nc.vector.tensor_tensor(h[r][:, cols], gelu_h[r][:, cols], up, ALU.mult)
                    ins.then_inc(h_done, 1)

            def rest_h(n, r, parts=1):
                for i, cols in enumerate(split(parts)):
                    dve.wait_ge(h_hi_done, n + 1 + i)
                    nc.vector.tensor_tensor(h_lo[r][:, cols], h[r][:, cols], h_hi[r][:, cols].bitcast(F32),
                                            ALU.subtract).then_inc(h_lo_done, 1)

            def residual1(b):
                dve.wait_ge(down_done, (b + 1) * STEPS)
                nc.vector.tensor_tensor(row(x, b), out1_ps[:, 0:S], row(x1, b), ALU.add).then_inc(y_done, 1)

            def layer1(b, odd, first=False, residual=True, with0=True, last=False):
                for s in range(STEPS):
                    if last and s == STEPS - 2:
                        rest_h(b * STEPS + s, s % H_RING)
                        product(b * STEPS + s + 1, b, s + 1, HALF)
                    elif last and s == STEPS - 1:
                        rest_h(b * STEPS + s, s % H_RING, HALF)
                    else:
                        if s < STEPS - 1:
                            product(b * STEPS + s + 1, b, s + 1)
                        else:
                            product((b + 1) * STEPS, b + 1, 0)
                        rest_h(b * STEPS + s, s % H_RING)
                    if s == 0 and not first:
                        residual1(b - 1)
                    if first and s == 0:
                        weigh()
                    if residual:
                        if s == (X_HI_AT if first else RESIDUAL_AT):
                            residual0(b + 1)
                        if s == X_HI_AT:
                            round_x1(b + 1)
                        if s == X_LO_AT:
                            rest_x1(b + 1)
                    if with0:
                        if s == BIAS_AT:
                            copy_bias(b + AHEAD, odd)
                        if s == SIGMOID_AT:
                            sigmoid(b + AHEAD)
                        if s == SILU_AT:
                            silu(b + AHEAD)
                        if s == PRODUCT_AT:
                            product0(b + AHEAD)
                        if s == REST_AT:
                            rest_h0(b + AHEAD)

            softmax_sum()
            split_up_gate0(0)
            copy_bias(0, 0)
            split_up_gate0(1)
            product0(0)
            copy_bias(1, 1)
            rest_h0_first(0)
            residual0(0)
            round_x1(0)
            rest_x1(0)
            product0(1)
            round_shared(2)
            probabilities()
            product(0, 0, 0)
            rest_h0_first(1)
            layer1(0, 0, first=True)
            with dve.Fori(1, LOOP_END, 2) as b:
                layer1(b, 1)
                layer1(b + 1, 0)
            for b in range(LOOP_END, B):
                layer1(b, b % 2, residual=b < B - 1, with0=b + AHEAD < B, last=b == B - 1)
            residual1(B - 1)

        @block.tensor
        def _(pe):
            def product3(out, w_hi, w_lo, m_hi, m_lo, start, stop, m_lo_ready=None):
                nc.tensor.matmul(out, w_hi, m_hi, start=start, stop=False)
                nc.tensor.matmul(out, w_lo, m_hi, start=False, stop=False)
                if m_lo_ready:
                    pe.wait_ge(*m_lo_ready)
                return nc.tensor.matmul(out, w_hi, m_lo, start=False, stop=stop)

            def product3_pair(sides, w_hi, w_lo, m_hi, m_lo, late):
                what, *lo_ready = late
                for bank, at, _ in sides:
                    cols = slice(at, at + P)
                    nc.tensor.matmul(chunk(bank, 0), w_hi[:, cols], m_hi, start=True, stop=False)
                    if what == "w":
                        nc.tensor.matmul(chunk(bank, 0), w_hi[:, cols], m_lo, start=False, stop=False)
                    else:
                        nc.tensor.matmul(chunk(bank, 0), w_lo[:, cols], m_hi, start=False, stop=False)
                pe.wait_ge(*lo_ready)
                for bank, at, ready in sides:
                    cols = slice(at, at + P)
                    if what == "w":
                        nc.tensor.matmul(chunk(bank, 0), w_lo[:, cols], m_hi, start=False, stop=True)
                    else:
                        nc.tensor.matmul(chunk(bank, 0), w_hi[:, cols], m_lo, start=False, stop=True)
                    cols = slice(at + P, at + 2 * P)
                    product3(chunk(bank, 1), w_hi[:, cols], w_lo[:, cols], m_hi, m_lo, True, True).then_inc(ready, 1)

            def wait_w0(b, n):
                if isinstance(b, int) and b < AHEAD:
                    pe.wait_ge((up_gate0_lo_first, down0_lo_first)[n], b + 1)
                else:
                    pe.wait_ge(w0_lo_done, (b - AHEAD) * 2 + n + 1)

            def up0_first():
                pe.wait_ge(x_lo_first, 1)
                pe.wait_ge(up_gate0_hi_first, 1)
                product3_pair(tuple(zip(banks0(0), (UP0, GATE0), (up0_ready, gate0_ready))), w0_hi[0], w0_lo[0],
                              row(x_hi, 0), row(x_lo, 0), ("w", up_gate0_lo_first, 1))

            def up0(b):
                j = slot0(b)
                wait_w0(b, 0)
                for bank, at, ready in zip(banks0(b), (UP0, GATE0), (up0_ready, gate0_ready)):
                    for c in range(C0):
                        cols = slice(at + c * P, at + (c + 1) * P)
                        last = product3(chunk(bank, c), w0_hi[j][:, cols], w0_lo[j][:, cols],
                                        row(x_hi, b), row(x_lo, b), True, True)
                    last.then_inc(ready, 1)

            def down0(b):
                j = slot0(b)
                wait_w0(b, 1)
                first = isinstance(b, int) and b < AHEAD
                if not first:
                    pe.wait_ge(h0_lo_done, (b + 1) * C0)
                for c in range(C0):
                    if first:
                        pe.wait_ge(h0_hi_done, b * C0 + c + 1)
                    cols = slice(DOWN0 + c * D, DOWN0 + (c + 1) * D)
                    last = product3(out0_ps[:, 0:S], w0_hi[j][:, cols], w0_lo[j][:, cols],
                                    chunk(h0_hi, c), chunk(h0_lo, c), c == 0, c == C0 - 1,
                                    (h0_lo_done, b * C0 + c + 1) if first else None)
                last.then_inc(out0_ready, 1)

            def up1(n, b, s, first=False):
                k, half = s * HALF // C1, s % (C1 // HALF)
                if s == 0:
                    if first:
                        pe.wait_ge(x1_hi_done, 1)
                    else:
                        pe.wait_ge(x1_lo_done, b + 1)
                if k == 0:
                    pe.wait_ge(w1_split[0][0], half + 1)
                elif half == 0:
                    pe.wait_ge(w1_split[k][0], b + 1)
                if not first:
                    pe.wait_ge(gelu_done, n - PS_RING + 1)
                    pe.wait_ge(h_done, n - PS_RING + 1)
                gate = half * 2 * HALF * P
                sides = ((gate1_ps[s % PS_RING], gate, gate1_ready),
                         (up1_ps[s % PS_RING], gate + HALF * P, up1_ready))
                if first and s == 0:
                    product3_pair(sides, w1_hi[k], w1_lo[k], row(x1_hi, b), row(x1_lo, b), ("m", x1_lo_done, 1))
                    return
                for bank, at, ready in sides:
                    for c in range(HALF):
                        lo = at + c * P
                        last = product3(chunk(bank, c), w1_hi[k][:, lo:lo + P], w1_lo[k][:, lo:lo + P],
                                        row(x1_hi, b), row(x1_lo, b), True, True)
                    last.then_inc(ready, 1)

            def down1(n, b, s, first=False, parts=1):
                r, k, half = s % H_RING, s * HALF // C1, s % (C1 // HALF)
                if s == 0 and not first:
                    pe.wait_ge(y_done, b)
                if half == 0:
                    pe.wait_ge(w1_split[k][1], b + 1 if k else 1)
                if parts == 1:
                    pe.wait_ge(h_lo_done, n + 1)
                for c in range(HALF):
                    if parts == HALF:
                        pe.wait_ge(h_hi_done, n + 1 + c)
                    lo = DOWN1 + (half * HALF + c) * D
                    last = product3(out1_ps[:, 0:S], w1_hi[k][:, lo:lo + D], w1_lo[k][:, lo:lo + D],
                                    chunk(h_hi[r], c), chunk(h_lo[r], c),
                                    s == 0 and c == 0, s == STEPS - 1 and c == HALF - 1,
                                    (h_lo_done, n + 1 + c) if parts == HALF else None)
                last.then_inc(down_done, 1)

            def layer1(b, first=False, with0=True, last=False):
                for s in range(STEPS):
                    ahead = s + LAG
                    if ahead < STEPS:
                        up1(b * STEPS + ahead, b, ahead)
                    elif not last:
                        up1((b + 1) * STEPS + ahead - STEPS, b + 1, ahead - STEPS)
                    if first and s == 0:
                        down0(1)
                    down1(b * STEPS + s, b, s, first, HALF if last and s == STEPS - 1 else 1)
                    if s == UP_AT and with0:
                        if not first:
                            pe.wait_ge(x_lo_done, b)
                        up0(b + AHEAD)
                    if s == DOWN_AT and with0:
                        down0(b + AHEAD)

            pe.wait_ge(zeroed, 1)

            def keep_warm(n):
                for _ in range(n):
                    nc.tensor.matmul(out1_ps[:, :], zeros_w[:, :], zeros_m[:, :], start=True, stop=True)

            keep_warm(12)
            up0_first()
            up0(1)
            down0(0)
            keep_warm(5)
            up1(0, 0, 0, first=True)
            pe.wait_ge(silu0_first, AHEAD * C0)
            pe.wait_ge(h0_done, AHEAD * C0)
            up1(1, 0, 1, first=True)
            layer1(0, first=True)
            with pe.Fori(1, B - AHEAD) as b:
                layer1(b)
            for b in range(B - AHEAD, B):
                layer1(b, with0=False, last=b == B - 1)


def kernel(x, cond_8, L0_cond_W_up, L0_cond_b_up, L0_cond_W_gate, L0_cond_b_gate, L0_cond_W_down, L0_cond_b_down,
           L1_cond_skill_gate, L1_cond_skill_up, L1_cond_skill_down,
           L1_cond_shared_gate, L1_cond_shared_up, L1_cond_shared_down):
    import numpy as np
    import concourse.bacc as bacc
    from concourse.bass_utils import run_bass_kernel_spmd

    def chunks_to_columns(w, parts):
        *lead, rows, n = w.shape
        w = w.reshape(*lead, parts, rows // parts, n)
        return np.moveaxis(w, -3, -2).reshape(*lead, rows // parts, parts * n)

    x_t = np.ascontiguousarray(np.asarray(x).reshape(B * S, D).T)
    cond = np.ascontiguousarray(np.asarray(cond_8).reshape(B * E))
    w0 = np.concatenate([
        np.swapaxes(np.asarray(L0_cond_W_up), 1, 2),
        np.swapaxes(np.asarray(L0_cond_W_gate), 1, 2),
        chunks_to_columns(np.asarray(L0_cond_b_up)[:, :, None], C0),
        chunks_to_columns(np.asarray(L0_cond_b_gate)[:, :, None], C0),
        np.asarray(L0_cond_b_down)[:, :, None],
        chunks_to_columns(np.swapaxes(np.asarray(L0_cond_W_down), 1, 2), C0),
    ], axis=-1)

    def pack1(gate, up, down):
        gate, up, down, half = np.asarray(gate), np.asarray(up), np.asarray(down), HALF * P
        return np.concatenate([part[..., at:at + half] for at in range(0, H1, half) for part in (gate, up)]
                              + [chunks_to_columns(down, C1)], axis=-1)

    w1 = pack1(L1_cond_skill_gate, L1_cond_skill_up, L1_cond_skill_down)
    shared = pack1(L1_cond_shared_gate, L1_cond_shared_up, L1_cond_shared_down)
    arrays = {"x_t": x_t, "cond": cond, "w0": w0, "w1": w1, "shared": shared}
    arrays = {name: np.ascontiguousarray(a) for name, a in arrays.items()}

    nc = bacc.Bacc("TRN2", target_bir_lowering=False, num_devices=1)
    ins = [nc.dram_tensor(name, a.shape, mybir.dt.from_np(a.dtype), kind="ExternalInput").ap()
           for name, a in arrays.items()]
    out = nc.dram_tensor("out_t", (D, B * S), F32, kind="ExternalOutput").ap()
    program(nc, *ins, out)
    got = run_bass_kernel_spmd(nc, [arrays], core_ids=[0]).results[0]["out_t"]
    return np.ascontiguousarray(got.T).reshape(B, S, D)
```
